# Optimizing a Trainium2 kernel written in Bass

```python
import numpy as np
import jax
import jax.numpy as jnp

def _softmax(x, axis=-1):
    return jax.nn.softmax(x, axis=axis)

def _gelu(x):
    return jax.nn.gelu(x, approximate=True)

def _silu(x):
    return jax.nn.silu(x)

def _sigmoid(x):
    return jax.nn.sigmoid(x)

def _layernorm(x, axis=-1, eps=1e-05):
    m = jnp.mean(x, axis=axis, keepdims=True)
    v = jnp.var(x, axis=axis, keepdims=True)
    return (x - m) / jnp.sqrt(v + eps)

def _scatter_add(tgt, idx, src, axis=0):
    return tgt.at[idx].add(src)

def _segment_sum(src, seg, n):
    return jax.ops.segment_sum(src, seg, n)
kernel_name = 'mk_seq_preln_d1_jaxref_r8_5234fa'

def setup_inputs(seed: int=0):
    np.random.seed(seed)
    _w = jnp.asarray

    def _L0_attn_setup():
        import jax, jax.numpy as jnp
        import numpy as np
        DIM = 128
        NUM_HEADS = 16
        DIM_HEAD = 64
        INNER = NUM_HEADS * DIM_HEAD

        def rotate_half(t):
            x1, x2 = jnp.split(t, 2, axis=-1)
            return jnp.concatenate([-x2, x1], axis=-1)

        def rope_pos(n, d, dtype=jnp.float32):
            inv_freq = 1.0 / 10000.0 ** (jnp.arange(0, d, 2, dtype=jnp.float32) / d)
            freqs = jnp.arange(n, dtype=jnp.float32)[:, None] * inv_freq[None, :]
            return jnp.concatenate([freqs, freqs], axis=-1).astype(dtype)

        def apply_rope(pos, t):
            return t * jnp.cos(pos) + rotate_half(t) * jnp.sin(pos)
        key = jax.random.key(seed)
        k1, k2, k3, k4 = jax.random.split(key, 4)
        b, n = (2, 256)
        x = jax.random.normal(k1, (b, n, DIM), dtype=jnp.float32)
        s = DIM ** (-0.5)
        Wq = jax.random.normal(k2, (DIM, INNER), dtype=jnp.float32) * s
        Wkv = jax.random.normal(k3, (DIM, 2 * DIM_HEAD), dtype=jnp.float32) * s
        Wo = jax.random.normal(k4, (INNER, DIM), dtype=jnp.float32) * INNER ** (-0.5)
        return {'x': x, 'Wq': Wq, 'Wkv': Wkv, 'Wo': Wo}
    _L0_attn_in = _L0_attn_setup()

    def _L0_ffn_setup():
        import jax, jax.numpy as jnp
        import numpy as np
        E = 8
        TOPK = 2
        SCALE = 2.0
        key = jax.random.key(seed)
        ks = jax.random.split(key, 12)
        B, S, D, F, R = (2, 64, 128, 512, 16)
        w = lambda k, shp: jax.random.normal(k, shp, dtype=jnp.float32) * 0.02
        return {'hidden_states': jax.random.normal(ks[0], (B, S, D), dtype=jnp.float32), 'gate_w': w(ks[1], (E, D)), 'w_gate': w(ks[2], (F, D)), 'w_up': w(ks[3], (F, D)), 'w_down': w(ks[4], (D, F)), 'A1': w(ks[5], (E, R, D)), 'B1': w(ks[6], (E, F, R)), 'A3': w(ks[7], (E, R, D)), 'B3': w(ks[8], (E, F, R)), 'A2': w(ks[9], (E, R, F)), 'B2': w(ks[10], (E, D, R))}
    _L0_ffn_in = _L0_ffn_setup()
    _d = {'L0_attn_x': _L0_attn_in['x'], 'L0_attn_Wq': _L0_attn_in['Wq'], 'L0_attn_Wkv': _L0_attn_in['Wkv'], 'L0_attn_Wo': _L0_attn_in['Wo'], 'L0_ffn_gate_w': _L0_ffn_in['gate_w'], 'L0_ffn_w_gate': _L0_ffn_in['w_gate'], 'L0_ffn_w_up': _L0_ffn_in['w_up'], 'L0_ffn_w_down': _L0_ffn_in['w_down'], 'L0_ffn_A1': _L0_ffn_in['A1'], 'L0_ffn_B1': _L0_ffn_in['B1'], 'L0_ffn_A3': _L0_ffn_in['A3'], 'L0_ffn_B3': _L0_ffn_in['B3'], 'L0_ffn_A2': _L0_ffn_in['A2'], 'L0_ffn_B2': _L0_ffn_in['B2']}
    _x0 = _d['L0_attn_x']
    _d['L0_attn_x'] = jax.random.normal(jax.random.fold_in(jax.random.key(seed), 1), (8, 512, 128), dtype=_x0.dtype)
    del _x0
    return _d

def reference(L0_attn_x, L0_attn_Wq, L0_attn_Wkv, L0_attn_Wo, L0_ffn_gate_w, L0_ffn_w_gate, L0_ffn_w_up, L0_ffn_w_down, L0_ffn_A1, L0_ffn_B1, L0_ffn_A3, L0_ffn_B3, L0_ffn_A2, L0_ffn_B2):

    def _L0_attn_ref(x, Wq, Wkv, Wo):
        import jax, jax.numpy as jnp
        import numpy as np
        DIM = 128
        NUM_HEADS = 16
        DIM_HEAD = 64
        INNER = NUM_HEADS * DIM_HEAD

        def rotate_half(t):
            x1, x2 = jnp.split(t, 2, axis=-1)
            return jnp.concatenate([-x2, x1], axis=-1)

        def rope_pos(n, d, dtype=jnp.float32):
            inv_freq = 1.0 / 10000.0 ** (jnp.arange(0, d, 2, dtype=jnp.float32) / d)
            freqs = jnp.arange(n, dtype=jnp.float32)[:, None] * inv_freq[None, :]
            return jnp.concatenate([freqs, freqs], axis=-1).astype(dtype)

        def apply_rope(pos, t):
            return t * jnp.cos(pos) + rotate_half(t) * jnp.sin(pos)
        b, n, _ = x.shape
        scale = DIM_HEAD ** (-0.5)
        q = x @ Wq
        kv = x @ Wkv
        k, v = jnp.split(kv, 2, axis=-1)
        q = q.reshape(b, n, NUM_HEADS, DIM_HEAD).transpose(0, 2, 1, 3)
        pos = rope_pos(n, DIM_HEAD, x.dtype)
        q = apply_rope(pos, q)
        k = apply_rope(pos, k)
        q = q * scale
        sim = jnp.einsum('bhid,bjd->bhij', q, k)
        causal = jnp.triu(jnp.ones((n, n), dtype=bool), k=1)
        neg = -jnp.finfo(sim.dtype).max
        sim = jnp.where(causal, neg, sim)
        sim = sim - jnp.max(sim, axis=-1, keepdims=True)
        attn = jax.nn.softmax(sim, axis=-1)
        out = jnp.einsum('bhij,bjd->bhid', attn, v)
        out = out.transpose(0, 2, 1, 3).reshape(b, n, INNER)
        return out @ Wo

    def _L0_ffn_ref(hidden_states, gate_w, w_gate, w_up, w_down, A1, B1, A3, B3, A2, B2):
        import jax, jax.numpy as jnp
        import numpy as np
        E = 8
        TOPK = 2
        SCALE = 2.0
        B, S, D = hidden_states.shape
        x = hidden_states.reshape(-1, D)
        N = x.shape[0]
        probs = jax.nn.softmax(x @ gate_w.T, axis=-1)
        vals, idx = jax.lax.top_k(probs, TOPK)
        rw = vals / jnp.sum(vals, axis=-1, keepdims=True)
        weight = jnp.zeros((N, E), x.dtype).at[jnp.arange(N)[:, None], idx].add(rw)
        common_w1 = x @ w_gate.T
        common_w3 = x @ w_up.T
        d1 = jnp.einsum('enr,efr->enf', jnp.einsum('nd,erd->enr', x, A1), B1) * SCALE
        d3 = jnp.einsum('enr,efr->enf', jnp.einsum('nd,erd->enr', x, A3), B3) * SCALE
        act = jax.nn.silu(common_w1[None] + d1) * (common_w3[None] + d3)
        out = jnp.einsum('ne,enf->nf', weight, act) @ w_down.T
        z = jnp.einsum('enf,erf->enr', act, A2)
        out = out + jnp.einsum('ne,enr,edr->nd', weight, z, B2) * SCALE
        return out.reshape(B, S, D)
    x = L0_attn_x
    x = x + _L0_attn_ref(_layernorm(x, axis=-1), L0_attn_Wq, L0_attn_Wkv, L0_attn_Wo)
    x = x + _L0_ffn_ref(_layernorm(x, axis=-1), L0_ffn_gate_w, L0_ffn_w_gate, L0_ffn_w_up, L0_ffn_w_down, L0_ffn_A1, L0_ffn_B1, L0_ffn_A3, L0_ffn_B3, L0_ffn_A2, L0_ffn_B2)
    return x

_drawn_inputs = setup_inputs


def setup_inputs(seed=0):
    import zlib

    import numpy as np

    out = dict(_drawn_inputs(seed))
    spreads = {}
    factors = {'L0_ffn_gate_w': 8.0,
     'L0_ffn_w_gate': 4.799,
     'L0_ffn_w_up': 4.782,
     'L0_ffn_w_down': 4.786,
     'L0_ffn_A1': 8.0,
     'L0_ffn_B1': 8.0,
     'L0_ffn_A3': 8.0,
     'L0_ffn_B3': 8.0,
     'L0_ffn_A2': 8.0,
     'L0_ffn_B2': 8.0}
    for name, (base, spread) in spreads.items():
        noise = np.random.default_rng([zlib.crc32(name.encode()), seed]).standard_normal(out[name].shape)
        drawn = base * np.exp(spread * noise) if base else spread * noise
        out[name] = jnp.asarray(drawn.astype(out[name].dtype))
    for name, factor in factors.items():
        out[name] = (out[name] * factor).astype(out[name].dtype)
    return out
```

```python
import concourse.bass as bass
from concourse import mybir
from contextlib import ExitStack
import numpy as np

fp32 = mybir.dt.float32
f32r = mybir.dt.float32r
bf16 = mybir.dt.bfloat16
u32 = mybir.dt.uint32
ALU = mybir.AluOpType
ACT = mybir.ActivationFunctionType
AX = mybir.AxisListType

P = 128
B, S, D = 8, 512, 128
NT = S // P
TILES = B * NT
H, DH = 16, 64
HALF = DH // 2
PAIRS = H // 2
NPAIR = B * PAIRS
ITER = NPAIR // 2
TURNS = PAIRS // 2
E, F, R = 8, 512, 16
FC = F // P
EPS = 1e-5
LORA_SCALE = 2.0
MASKED = -1e30


def wait_reuse(engine, semaphore, count):
    if not isinstance(count, int) or count > 0:
        engine.wait_ge(semaphore, count)


def row_scales(nc, dve, act, stats, mean, rstd, tmp, done, signals):
    step, var_ready, root_ready = signals

    def vector_part():
        n = [0]

        def then(ins):
            n[0] += 1
            ins.then_inc(step, 1)
            dve.wait_ge(step, n[0])

        me, m2e = stats[:, :, 1], stats[:, :, 2]
        mo, m2o = stats[:, :, 4], stats[:, :, 5]
        var, a, b = tmp[:, 0, :], tmp[:, 1, :], tmp[:, 2, :]
        then(nc.vector.tensor_tensor(a, me, mo, ALU.add))
        then(nc.vector.tensor_scalar(mean, a, 0.5, None, ALU.mult))
        then(nc.vector.tensor_tensor(a, me, mo, ALU.subtract))
        then(nc.vector.tensor_tensor(a, a, a, ALU.mult))
        then(nc.vector.tensor_tensor(b, m2e, m2o, ALU.add))
        then(nc.vector.tensor_scalar(b, b, 1.0 / D, EPS, ALU.mult, ALU.add))
        nc.vector.scalar_tensor_tensor(out=var, in0=a, scalar=0.25, in1=b, op0=ALU.mult,
                                       op1=ALU.add).then_inc(var_ready, 1)
        dve.wait_ge(root_ready, 1)
        then(nc.vector.reciprocal(a, tmp[:, 3, :]))
        then(nc.vector.tensor_tensor(b, a, a, ALU.mult))
        then(nc.vector.tensor_tensor(b, b, var, ALU.mult))
        then(nc.vector.tensor_scalar(b, b, -0.5, 1.5, ALU.mult, ALU.add))
        nc.vector.tensor_tensor(rstd, a, b, ALU.mult).then_inc(done, 1)
        dve.wait_ge(done, 1)

    def scalar_part():
        act.wait_ge(var_ready, 1)
        nc.scalar.activation(tmp[:, 3, :], tmp[:, 0, :], ACT.Sqrt).then_inc(root_ready, 1)

    return vector_part, scalar_part


def attention_block(nc, x_all, x_dram, wq_dram, wkv_dram, wo_dram, rope_q_dram, rope_k_dram,
                    mask_dram):
    with ExitStack() as ctx:
        def sb(name, shape, dt):
            return ctx.enter_context(nc.sbuf_tensor(name, shape, dt))

        def sem(name):
            return ctx.enter_context(nc.semaphore(name))

        ident = sb("ident", [P, P], fp32)
        ident_bf = sb("ident_bf", [P, P], bf16)
        mask_bf = sb("mask_bf", [P, P], bf16)
        rope_q = sb("rope_q", [P, 2, NT * P], fp32)
        rope_k = sb("rope_k", [P, 2, S], fp32)
        wq = sb("wq", [P, H * DH], fp32)
        wkv = sb("wkv", [P, 2 * DH], fp32)
        wk_twice = sb("wk_twice", [P, 2, DH], fp32)
        wk_rot = sb("wk_rot", [P, 2, DH], fp32)
        wo = sb("wo", [P, PAIRS, D], fp32)
        stats = sb("stats1", [P, TILES, 6], fp32)
        mean = sb("mean1", [P, TILES], fp32)
        rstd = sb("rstd1", [P, TILES], fp32)
        ln_tmp = sb("ln_tmp1", [P, 4, TILES], fp32)
        xnT_all = sb("xnT_all", [P, B * S], fp32)
        k_hi = sb("k_hi", [P, B * S], f32r)
        k_lo = sb("k_lo", [P, B * S], f32r)
        v_all = sb("v_all", [P, B * NT * DH], fp32)
        xn = sb("xn1", [P, NT, D], fp32)
        xnT = sb("xnT1", [P, S], fp32)
        k_cos = sb("k_cos", [P, S], fp32)
        k_sin = sb("k_sin", [P, S], fp32)
        k_rot = sb("k_rot", [P, S], fp32)
        x_cur = [sb(f"x_cur{i}", [P, S], fp32) for i in range(2)]
        v_cur = [sb(f"v_cur{i}", [P, NT, DH], fp32) for i in range(2)]
        q_cos = sb("q_cos", [P, NT * 2, DH], fp32)
        q_sin = sb("q_sin", [P, NT * 2, DH], fp32)
        q_rot = sb("q_rot", [P, NT * 2, DH], fp32)
        q_split = [sb(f"q_split{i}", [P, 2, S], f32r) for i in range(2)]
        neg_max = sb("neg_max", [P, NT, 2], fp32)
        row_sum = sb("row_sum", [P, NT, 2], fp32)
        row_inv = sb("row_inv", [P, NT, 2], fp32)
        probs = [sb(f"probs{i}", [P, 2, (i + 1) * P], fp32) for i in range(NT)]
        probs_T = [sb(f"probs_T{i}", [P, 2, NT, S], fp32) for i in range(2)]
        heads_T = sb("heads_T", [P, S], fp32)

        scores = ctx.enter_context(nc.psum_tensor("scores", [P, 2, 2, S], fp32))
        turned = ctx.enter_context(nc.psum_tensor("turned", [P, 2, S], fp32))
        queries = ctx.enter_context(nc.psum_tensor("queries", [P, S], fp32))
        mixed = ctx.enter_context(nc.psum_tensor("mixed", [P, S], fp32))

        x_loaded = [sem(f"x_loaded{b}") for b in range(B)]
        w_loaded, rope_loaded, wqo_loaded = sem("w_loaded"), sem("rope_loaded"), sem("wqo_loaded")
        ident_ready = sem("ident_ready")
        wk_ready = sem("wk_ready")
        stats_ready = sem("stats_ready")
        ln_signals = (sem("ln_step1"), sem("var_ready1"), sem("root_ready1"))
        ln_ready = sem("ln_ready1")
        xn_ready, xnT_in_psum, xnT_ready = sem("xn_ready1"), sem("xnT_in_psum1"), sem("xnT_ready1")
        k_in_psum, v_in_psum = sem("k_in_psum"), sem("v_in_psum")
        k_scaled, k_added, k_high, k_ready, v_ready = (sem(n) for n in
            ("k_scaled", "k_added", "k_high", "k_ready", "v_ready"))
        x_cur_loaded = [sem(f"x_cur_loaded{i}") for i in range(2)]
        v_cur_loaded = [sem(f"v_cur_loaded{i}") for i in range(2)]
        q_in_psum, q_scaled, q_rotated, q_turned, q_high, q_ready = (sem(n) for n in
            ("q_in_psum", "q_scaled", "q_rotated", "q_turned", "q_high", "q_ready"))
        scores_ready, max_ready, exp_done, inv_ready, probs_ready = (sem(n) for n in
            ("scores_ready", "max_ready", "exp_done", "inv_ready", "probs_ready"))
        probs_turned, probs_T_ready, heads_in_psum, heads_T_ready, wo_done, x_added = (sem(n) for n in
            ("probs_turned", "probs_T_ready", "heads_in_psum", "heads_T_ready", "wo_done", "x_added"))

        block = ctx.enter_context(nc.Block())

        @block.sync
        def _(sp):
            for b in range(0, B, 2):
                sp.dma_start(x_all[:, b * NT:(b + 1) * NT, :],
                             x_dram[b].rearrange("(i p) d -> p i d", p=P)).then_inc(x_loaded[b], 16)
            sp.dma_start(wkv[:, :], wkv_dram).then_inc(w_loaded, 16)
            sp.dma_start(rope_k[:, :, :], rope_k_dram).then_inc(rope_loaded, 16)
            sp.dma_start(mask_bf[:, :], mask_dram).then_inc(rope_loaded, 16)
            sp.dma_start(wq[:, :], wq_dram).then_inc(wqo_loaded, 16)
            sp.dma_start(rope_q[:, :, :], rope_q_dram).then_inc(wqo_loaded, 16)
            sp.dma_start(wo[:, :, :], wo_dram.rearrange("(g p) d -> p g d", p=P)).then_inc(wqo_loaded, 16)
            sp.wait_ge(xnT_ready, 2 * B)
            sp.wait_ge(v_ready, B)

            def load_x(t, half):
                sp.dma_start(x_cur[half][:, :], xnT_all[:, bass.ds((t // TURNS) * S, S)]) \
                    .then_inc(x_cur_loaded[half], 16)

            def load_v(t, half):
                sp.dma_start(v_cur[half][:, :, :].rearrange("p i d -> p (i d)"),
                             v_all[:, bass.ds((t // TURNS) * (NT * DH), NT * DH)]) \
                    .then_inc(v_cur_loaded[half], 16)

            load_x(0, 0)
            load_x(0, 1)
            load_v(0, 0)
            sp.wait_ge(q_in_psum, 1)
            load_x(1, 0)
            load_v(0, 1)
            with sp.Fori(1, ITER - 1) as t:
                sp.wait_ge(q_in_psum, 2 * t)
                load_x(t, 1)
                sp.wait_ge(heads_in_psum, 2 * t - 1)
                load_v(t, 0)
                sp.wait_ge(q_in_psum, 2 * t + 1)
                load_x(t + 1, 0)
                sp.wait_ge(heads_in_psum, 2 * t)
                load_v(t, 1)
            sp.wait_ge(q_in_psum, NPAIR - 2)
            load_x(ITER - 1, 1)
            sp.wait_ge(heads_in_psum, NPAIR - 3)
            load_v(ITER - 1, 0)
            sp.wait_ge(heads_in_psum, NPAIR - 2)
            load_v(ITER - 1, 1)

        @block.gpsimd
        def _(pool):
            pool.memset(ident[:, :], 1.0).then_inc(ident_ready, 1)
            pool.memset(ident_bf[:, :], 1.0).then_inc(ident_ready, 1)
            pool.wait_ge(ident_ready, 2)
            for m in (ident, ident_bf):
                pool.affine_select(out=m[:, :], in_=m[:, :], compare_op=ALU.is_equal, fill=0.0, base=0,
                                   pattern=[[-1, P]], channel_multiplier=1).then_inc(ident_ready, 1)
            def add_key_parts(b):
                pool.wait_ge(k_scaled, b + 1)
                wait_reuse(pool, k_ready, b)
                pool.tensor_tensor(k_rot[:, :], k_cos[:, :], k_sin[:, :], ALU.add).then_inc(k_added, 1)

            add_key_parts(0)
            with pool.Fori(1, B) as b:
                add_key_parts(b)

            def rotate(g):
                pool.wait_ge(q_scaled, g + 1)
                wait_reuse(pool, q_turned, g)
                pool.tensor_tensor(q_rot[:, :, 0:HALF], q_cos[:, :, 0:HALF], q_sin[:, :, HALF:DH], ALU.add)
                pool.tensor_tensor(q_rot[:, :, HALF:DH], q_cos[:, :, HALF:DH], q_sin[:, :, 0:HALF], ALU.add) \
                    .then_inc(q_rotated, 1)

            def normalise(n, i):
                count = n + 1 if isinstance(n, int) else pool.to_reg(n + 1)
                pool.wait_ge(ident_ready, 4)
                pool.wait_ge(inv_ready, count)
                for h in range(2):
                    pool.tensor_scalar(probs[i][:, h, :], probs[i][:, h, :], row_inv[:, i, h:h + 1], 1.0,
                                       ALU.mult, ALU.mult).then_inc(probs_ready, 1)

            def turn(t, first, last):
                for half in range(2):
                    for i in range(NT):
                        if i == 1 and not (last and half == 1):
                            rotate(2 * t + half + 1)
                        if not (first and half == 0 and i == 0):
                            normalise(8 * t + 4 * half + i - 1, (i - 1) % NT)

            rotate(0)
            turn(0, True, False)
            with pool.Fori(1, ITER - 1) as t:
                turn(t, False, False)
            turn(ITER - 1, False, True)
            normalise(8 * ITER - 1, NT - 1)

        @block.vector
        def _(dve):
            for b in range(B):
                dve.wait_ge(x_loaded[b], 16)
                for i in range(NT):
                    last = nc.vector.bn_stats(stats[:, b * NT + i, :], x_all[:, b * NT + i, :])
            last.then_inc(stats_ready, 1)
            dve.wait_ge(stats_ready, 1)
            row_scales(nc, dve, None, stats, mean[:, :], rstd[:, :], ln_tmp, ln_ready, ln_signals)[0]()
            dve.wait_ge(w_loaded, 16)
            wk = wkv[:, 0:DH]
            for c in range(2):
                nc.vector.tensor_copy(wk_twice[:, c, :], wk)
                nc.vector.tensor_copy(wk_rot[:, c, 0:HALF], wk[:, HALF:DH])
                last = nc.vector.tensor_copy(wk_rot[:, c, HALF:DH], wk[:, 0:HALF])
            last.then_inc(wk_ready, 1)

            def normalise_tokens(b):
                wait_reuse(dve, xnT_in_psum, b)
                for i in range(NT):
                    last = nc.vector.tensor_scalar(
                        xn[:, i, :], x_all[:, bass.ds(b * NT + i, 1), :].rearrange("p i d -> p (i d)"),
                        mean[:, bass.ds(b * NT + i, 1)], rstd[:, bass.ds(b * NT + i, 1)],
                        ALU.subtract, ALU.mult)
                last.then_inc(xn_ready, 1)

            def rotate_keys(b):
                here = bass.ds(b * S, S)
                dve.wait_ge(k_in_psum, b + 1)
                nc.vector.tensor_tensor(k_cos[:, :], queries[:, :], rope_k[:, 0, :], ALU.mult)
                nc.vector.tensor_tensor(k_sin[:, :], mixed[:, :], rope_k[:, 1, :], ALU.mult) \
                    .then_inc(k_scaled, 1)
                dve.wait_ge(k_added, b + 1)
                nc.vector.tensor_copy(k_hi[:, here], k_rot[:, :]).then_inc(k_high, 1)
                dve.wait_ge(k_high, b + 1)
                nc.vector.tensor_tensor(k_lo[:, here], k_rot[:, :], k_hi[:, here].bitcast(fp32),
                                        ALU.subtract).then_inc(k_ready, 1)

            normalise_tokens(0)
            dve.wait_ge(rope_loaded, 32)
            with dve.Fori(0, B - 1) as b:
                normalise_tokens(b + 1)
                rotate_keys(b)
            rotate_keys(B - 1)

            def scale_queries(g):
                dve.wait_ge(q_in_psum, g + 1)
                wait_reuse(dve, q_rotated, g)
                q = queries[:, :].rearrange("p (i d) -> p i d", d=DH)
                cos, sin = (rope_q[:, c, :].rearrange("p (i d) -> p i d", d=DH) for c in range(2))
                nc.vector.tensor_tensor(q_cos[:, :, :], q, cos, ALU.mult)
                nc.vector.tensor_tensor(q_sin[:, :, :], q, sin, ALU.mult).then_inc(q_scaled, 1)

            def split_queries(g, half):
                q = q_split[half]
                dve.wait_ge(q_high, 2 * g + 1)
                nc.vector.tensor_tensor(q[DH:P, 0, :], queries[0:DH, :], q[0:DH, 0, :].bitcast(fp32),
                                        ALU.subtract)
                dve.wait_ge(q_high, 2 * g + 2)
                nc.vector.tensor_tensor(q[0:DH, 1, :], queries[DH:P, :], q[DH:P, 1, :].bitcast(fp32),
                                        ALU.subtract).then_inc(q_ready, 1)

            def row_max(n, slot, i):
                dve.wait_ge(scores_ready, n + 1)
                nc.vector.tensor_reduce(out=neg_max[:, i, :], in_=scores[:, slot, :, 0:(i + 1) * P],
                                        op=ALU.max, axis=AX.X, negate=True).then_inc(max_ready, 1)

            def row_reciprocal(n, i):
                dve.wait_ge(exp_done, 2 * n + 2)
                nc.vector.reciprocal(row_inv[:, i, :], row_sum[:, i, :]).then_inc(inv_ready, 1)

            def add_to_x(g, b):
                here = x_all[:, bass.ds(b * NT, NT), :]
                dve.wait_ge(wo_done, g + 1)
                nc.vector.tensor_tensor(here, mixed[:, :].rearrange("p (i d) -> p i d", d=D), here,
                                        ALU.add).then_inc(x_added, 1)

            def copy_heads(g):
                dve.wait_ge(heads_in_psum, g + 1)
                nc.vector.tensor_copy(heads_T[:, :], mixed[:, :]).then_inc(heads_T_ready, 1)

            def turn(t, first, last):
                for half in range(2):
                    g = 2 * t + half
                    for i in range(NT):
                        n = 8 * t + 4 * half + i
                        row_max(n, i % 2, i)
                        if not (first and half == 0 and i == 0):
                            row_reciprocal(n - 1, (i - 1) % NT)
                        if i == 0 and not (last and half == 1):
                            scale_queries(g + 1)
                        if i == 1 and not first:
                            add_to_x(g - 2, (t - 1) // TURNS)
                        if i == 3 and not (last and half == 1):
                            split_queries(g + 1, 1 - half)
                        if i == 3 and not (first and half == 0):
                            copy_heads(g - 1)

            scale_queries(0)
            split_queries(0, 0)
            turn(0, True, False)
            with dve.Fori(1, ITER - 1) as t:
                turn(t, False, False)
            turn(ITER - 1, False, True)
            row_reciprocal(8 * ITER - 1, NT - 1)
            add_to_x(NPAIR - 2, B - 1)
            copy_heads(NPAIR - 1)
            add_to_x(NPAIR - 1, B - 1)

        @block.scalar
        def _(act):
            for b in range(1, B, 2):
                act.dma_start(x_all[:, b * NT:(b + 1) * NT, :],
                              x_dram[b].rearrange("(i p) d -> p i d", p=P)).then_inc(x_loaded[b], 16)
            row_scales(nc, None, act, stats, mean[:, :], rstd[:, :], ln_tmp, ln_ready, ln_signals)[1]()
            def copy_prepared(b):
                wait_reuse(act, v_in_psum, b)
                act.wait_ge(xnT_in_psum, b + 1)
                nc.scalar.activation(xnT[:, :], turned[:, 0, :], ACT.Copy).then_inc(xnT_ready, 1)
                nc.scalar.activation(xnT_all[:, bass.ds(b * S, S)], turned[:, 0, :], ACT.Copy) \
                    .then_inc(xnT_ready, 1)
                act.wait_ge(ln_signals[1], 1)
                act.wait_ge(v_in_psum, b + 1)
                nc.scalar.activation(v_all[:, bass.ds(b * (NT * DH), NT * DH)],
                                     scores[:, 0, 0, 0:NT * DH], ACT.Copy).then_inc(v_ready, 1)

            copy_prepared(0)
            with act.Fori(1, B) as b:
                copy_prepared(b)

            def high_queries(g, half):
                q = q_split[half]
                act.wait_ge(q_turned, g + 1)
                nc.scalar.activation(q[0:DH, 0, :], queries[0:DH, :], ACT.Copy).then_inc(q_high, 1)
                nc.scalar.activation(q[DH:P, 1, :], queries[DH:P, :], ACT.Copy).then_inc(q_high, 1)

            def exponents(n, slot, i, reused):
                for h in range(2):
                    act.wait_ge(max_ready, n + 1)
                    if reused and h == 0:
                        act.wait_ge(probs_turned, 2 * (n - 3))
                    nc.scalar.activation(probs[i][:, h, :], scores[:, slot, h, 0:(i + 1) * P], ACT.Exp,
                                         bias=neg_max[:, i, h:h + 1],
                                         accum_out=row_sum[:, i, h:h + 1]).then_inc(exp_done, 1)

            def copy_turned(m, i, half, g, reused):
                for h in range(2):
                    if reused and h == 0 and i == 0:
                        act.wait_ge(heads_in_psum, g - 1)
                    act.wait_ge(probs_turned, 2 * m + h + 1)
                    nc.scalar.activation(
                        probs_T[half][:, h, 0:i + 1, i * P:(i + 1) * P],
                        turned[:, h, 0:(i + 1) * P].rearrange("p (j q) -> p j q", q=P), ACT.Copy) \
                        .then_inc(probs_T_ready, 1)

            def turn(t, first, last):
                for half in range(2):
                    g = 2 * t + half
                    for i in range(NT):
                        n = 8 * t + 4 * half + i
                        exponents(n, i % 2, i, not (first and half == 0))
                        if i == 3:
                            copy_turned(n - 3, 0, half, g, not first)
                        elif not (first and half == 0):
                            copy_turned(n - 3, i + 1, 1 - half, g - 1, True)
                        if i == 2 and not (last and half == 1):
                            high_queries(g + 1, 1 - half)

            high_queries(0, 0)
            turn(0, True, False)
            with act.Fori(1, ITER - 1) as t:
                turn(t, False, False)
            turn(ITER - 1, False, True)
            for i in (1, 2, 3):
                copy_turned(8 * ITER - 4 + i, i, 1, NPAIR - 1, True)

        @block.tensor
        def _(pe):
            pe.wait_ge(ident_ready, 4)
            pe.wait_ge(wk_ready, 1)

            def transpose_tokens(b):
                wait_reuse(pe, xnT_ready, 2 * b)
                pe.wait_ge(xn_ready, b + 1)
                for i in range(NT):
                    last = nc.tensor.transpose(turned[:, 0, i * P:(i + 1) * P], xn[:, i, :], ident[:, :])
                last.then_inc(xnT_in_psum, 1)

            def keys_and_values(b):
                wait_reuse(pe, k_scaled, b)
                pe.wait_ge(xnT_ready, 2 * b + 1)
                nc.tensor.matmul(queries[:, :], wk_twice[:, :, :].rearrange("p c d -> p (c d)"), xnT[:, :],
                                 start=True, stop=True)
                nc.tensor.matmul(mixed[:, :], wk_rot[:, :, :].rearrange("p c d -> p (c d)"), xnT[:, :],
                                 start=True, stop=True).then_inc(k_in_psum, 1)
                wait_reuse(pe, v_ready, b)
                for i in range(NT):
                    last = nc.tensor.matmul(scores[:, 0, 0, i * DH:(i + 1) * DH], xnT[:, i * P:(i + 1) * P],
                                            wkv[:, DH:2 * DH], start=True, stop=True)
                last.then_inc(v_in_psum, 1)

            transpose_tokens(0)
            keys_and_values(0)
            transpose_tokens(1)
            with pe.Fori(1, B - 1) as b:
                keys_and_values(b)
                transpose_tokens(b + 1)
            keys_and_values(B - 1)

            def project_queries(g, t, half, pair):
                pe.wait_ge(x_cur_loaded[half], 16 * (t + 1))
                for i in range(NT):
                    last = nc.tensor.matmul(queries[:, i * P:(i + 1) * P], x_cur[half][:, i * P:(i + 1) * P],
                                            wq[:, bass.ds(pair * P, P)], start=True, stop=True)
                last.then_inc(q_in_psum, 1)

            def transpose_queries(g):
                pe.wait_ge(q_rotated, g + 1)
                for i in range(NT):
                    last = nc.tensor.transpose(queries[:, i * P:(i + 1) * P],
                                               q_rot[:, 2 * i:2 * i + 2, :].rearrange("p h d -> p (h d)"),
                                               ident[:, :])
                last.then_inc(q_turned, 1)

            def score(n, slot, i, half, b, reused):
                keys = (i + 1) * P
                if reused:
                    pe.wait_ge(exp_done, 2 * (n - 1))
                for h in range(2):
                    q = q_split[half][:, h, i * P:(i + 1) * P]
                    out = scores[:, slot, h, 0:keys]
                    nc.tensor.matmul(out, q, k_hi[:, bass.ds(b * S, keys)], start=True, stop=False)
                    nc.tensor.matmul(out, q, k_lo[:, bass.ds(b * S, keys)], start=False, stop=False)
                    last = nc.tensor.matmul(scores[:, slot, h, i * P:keys], ident_bf[:, :], mask_bf[:, :],
                                            start=False, stop=True)
                last.then_inc(scores_ready, 1)

            def turn_probs(m, i, reused):
                for h in range(2):
                    if reused:
                        pe.wait_ge(probs_T_ready, 2 * m - 1 + h)
                    pe.wait_ge(probs_ready, 2 * m + h + 1)
                    for j in range(i + 1):
                        last = nc.tensor.transpose(turned[:, h, j * P:(j + 1) * P],
                                                   probs[i][:, h, j * P:(j + 1) * P], ident[:, :])
                    last.then_inc(probs_turned, 1)

            def mix_values(g, t, half):
                pe.wait_ge(probs_T_ready, 8 * (g + 1))
                pe.wait_ge(v_cur_loaded[half], 16 * (t + 1))
                for j in range(NT):
                    for h in range(2):
                        last = nc.tensor.matmul(mixed[h * DH:(h + 1) * DH, j * P:S], v_cur[half][:, j, :],
                                                probs_T[half][:, h, j, j * P:S], start=(j == 0),
                                                stop=(j == NT - 1))
                last.then_inc(heads_in_psum, 1)

            def project_heads(g, pair):
                pe.wait_ge(heads_T_ready, g + 1)
                for i in range(NT):
                    last = nc.tensor.matmul(mixed[:, i * P:(i + 1) * P], heads_T[:, i * P:(i + 1) * P],
                                            wo[:, bass.ds(pair, 1), :].rearrange("p g d -> p (g d)"),
                                            start=True, stop=True)
                last.then_inc(wo_done, 1)

            def turn(t, first, last):
                first_pair = 2 * (t % TURNS)
                t_next, t_prev = t + 1, t - 1
                for half in range(2):
                    g = 2 * t + half
                    for i in range(NT):
                        n = 8 * t + 4 * half + i
                        if i == 0:
                            pe.wait_ge(q_ready, g + 1)
                        score(n, i % 2, i, half, t // TURNS, not (first and half == 0 and i < 2))
                        if i == 0 and not (last and half == 1):
                            if half == 0:
                                project_queries(g + 1, t, 1, first_pair + 1)
                            else:
                                project_queries(g + 1, t_next, 0, 2 * (t_next % TURNS))
                        if i == 0 and not first:
                            if half == 0:
                                project_heads(g - 2, 2 * (t_prev % TURNS))
                            else:
                                project_heads(g - 2, 2 * (t_prev % TURNS) + 1)
                        if i == 3:
                            turn_probs(n - 3, 0, not (first and half == 0))
                        elif not (first and half == 0):
                            turn_probs(n - 3, i + 1, True)
                        if i == 2 and not (last and half == 1):
                            transpose_queries(g + 1)
                        if i == 3 and not (first and half == 0):
                            if not first:
                                pe.wait_ge(x_added, g - 1)
                            mix_values(g - 1, t if half else t_prev, 1 - half)

            pe.wait_ge(k_ready, B)
            pe.wait_ge(v_ready, B)
            pe.wait_ge(xnT_ready, 2 * B)
            pe.wait_ge(wqo_loaded, 48)
            project_queries(0, 0, 0, 0)
            transpose_queries(0)
            turn(0, True, False)
            with pe.Fori(1, ITER - 1) as t:
                turn(t, False, False)
            turn(ITER - 1, False, True)
            project_heads(NPAIR - 2, PAIRS - 2)
            for i in (1, 2, 3):
                turn_probs(8 * ITER - 4 + i, i, True)
            pe.wait_ge(x_added, NPAIR - 1)
            mix_values(NPAIR - 1, ITER - 1, 1)
            project_heads(NPAIR - 1, PAIRS - 1)


def expert_weights_block(nc, w_hi, w_lo, w_dram, a_dram, b_dram):
    with ExitStack() as ctx:
        def sb(name, shape, dt=fp32):
            return ctx.enter_context(nc.sbuf_tensor(name, shape, dt))

        def sem(name):
            return ctx.enter_context(nc.semaphore(name))

        ident = sb("ident_w", [P, P])
        own = sb("own_rows", [P, E])
        w_rows = [sb(f"w_rows{m}", [P, FC, P]) for m in range(2)] + [sb("w_rows2", [P, F])]
        w_T = [sb(f"w_T{m}", [P, F]) for m in range(3)]
        a_rows = [sb(f"a_rows{m}", [P, D]) for m in range(2)] + [sb("a_rows2", [P, F])]
        b_rows = [sb(f"b_rows{m}", [P, FC, E, R]) for m in range(2)] + [sb("b_rows2", [P, E, R])]
        b_T = [sb(f"b_T{m}", [P, F]) for m in range(2)] + [sb("b_T2", [P, D])]
        a_own = [sb(f"a_own{m}", [P, D]) for m in range(2)] + [sb("a_own2", [P, F])]
        full = [sb(f"full{m}", [P, F]) for m in range(3)]
        psT = [ctx.enter_context(nc.psum_tensor(f"w_psT{m}", [P, F], fp32)) for m in range(3)]
        psU = [ctx.enter_context(nc.psum_tensor(f"w_psU{m}", [P, F], fp32)) for m in range(3)]
        loaded = [sem(f"w_rows_loaded{m}") for m in range(3)]
        ident_ready, own_ready = sem("ident_w_ready"), sem("own_ready")
        b_turned, b_T_ready, w_turned, w_T_ready = (sem(n) for n in
            ("b_turned", "b_T_ready", "w_turned", "w_T_ready"))
        own_masked, update_ready, full_ready, high_ready, low_ready = (sem(n) for n in
            ("own_masked", "update_ready", "full_ready", "high_ready", "low_ready"))
        block = ctx.enter_context(nc.Block())

        @block.sync
        def _(sp):
            for m in range(2):
                sp.dma_start(w_rows[m][:, :, :], w_dram[m].rearrange("(c p) d -> p c d", p=P)).then_inc(loaded[m], 16)
                sp.dma_start(a_rows[m][:, :], a_dram[m].rearrange("e r d -> (e r) d")).then_inc(loaded[m], 16)
                for c in range(FC):
                    sp.dma_start(b_rows[m][:, c, :, :],
                                 b_dram[m][:, c * P:(c + 1) * P, :].rearrange("e p r -> p e r")).then_inc(loaded[m], 16)

        @block.gpsimd
        def _(pool):
            pool.dma_start(w_rows[2][:, :], w_dram[2]).then_inc(loaded[2], 16)
            pool.dma_start(a_rows[2][:, :], a_dram[2].rearrange("e r f -> (e r) f")).then_inc(loaded[2], 16)
            pool.dma_start(b_rows[2][:, :, :], b_dram[2].rearrange("e d r -> d e r")).then_inc(loaded[2], 16)
            pool.memset(ident[:, :], 1.0).then_inc(ident_ready, 1)
            pool.memset(own[:, :], 1.0).then_inc(own_ready, 1)
            pool.wait_ge(ident_ready, 1)
            pool.affine_select(out=ident[:, :], in_=ident[:, :], compare_op=ALU.is_equal, fill=0.0, base=0,
                               pattern=[[-1, P]], channel_multiplier=1).then_inc(ident_ready, 1)
            pool.wait_ge(own_ready, 1)
            pool.affine_select(out=own[:, :], in_=own[:, :], compare_op=ALU.is_ge, fill=0.0, base=0,
                               pattern=[[-R, E]], channel_multiplier=1).then_inc(own_ready, 1)
            pool.wait_ge(own_ready, 2)
            pool.affine_select(out=own[:, :], in_=own[:, :], compare_op=ALU.is_ge, fill=0.0, base=R - 1,
                               pattern=[[R, E]], channel_multiplier=-1).then_inc(own_ready, 1)

        @block.tensor
        def _(pe):
            pe.wait_ge(ident_ready, 2)
            for m in range(3):
                pe.wait_ge(loaded[m], 16 * (2 + FC) if m < 2 else 48)
                for c in range(FC if m < 2 else 1):
                    rows = b_rows[m][:, c, :, :] if m < 2 else b_rows[m][:, :, :]
                    last = nc.tensor.transpose(psT[m][:, c * P:(c + 1) * P], rows.rearrange("p e r -> p (e r)"),
                                               ident[:, :])
                last.then_inc(b_turned, 1)
                for c in range(FC):
                    rows = w_rows[m][:, c, :] if m < 2 else w_rows[m][:, c * P:(c + 1) * P]
                    last = nc.tensor.transpose(psU[m][:, c * P:(c + 1) * P], rows, ident[:, :])
                last.then_inc(w_turned, 1)
            pe.wait_ge(b_T_ready, 3)
            pe.wait_ge(w_T_ready, 3)
            def update(e):
                for m in range(3):
                    wait_reuse(pe, full_ready, 3 * (e - 1) + m + 1)
                    pe.wait_ge(own_masked, 3 * e + m + 1)
                    if m < 2:
                        nc.tensor.matmul(psU[m][:, :], a_own[m][:, :], b_T[m][:, :], start=True, stop=True) \
                            .then_inc(update_ready, 1)
                    else:
                        for c in range(FC):
                            last = nc.tensor.matmul(psU[m][:, c * P:(c + 1) * P], a_own[m][:, c * P:(c + 1) * P],
                                                    b_T[m][:, :], start=True, stop=True)
                        last.then_inc(update_ready, 1)

            update(0)
            with pe.Fori(1, E) as e:
                update(e)

        @block.scalar
        def _(act):
            for m in range(3):
                act.wait_ge(b_turned, m + 1)
                cols = F if m < 2 else D
                nc.scalar.activation(b_T[m][:, :], psT[m][:, 0:cols], ACT.Copy).then_inc(b_T_ready, 1)
            with act.Fori(0, E) as e:
                for m in range(3):
                    act.wait_ge(full_ready, 3 * e + m + 1)
                    nc.scalar.activation(w_hi[m][:, bass.ds(e * F, F)], full[m][:, :], ACT.Copy) \
                        .then_inc(high_ready, 1)

        @block.vector
        def _(dve):
            for m in range(3):
                dve.wait_ge(w_turned, m + 1)
                nc.vector.tensor_copy(w_T[m][:, :], psU[m][:, :]).then_inc(w_T_ready, 1)
            dve.wait_ge(own_ready, 3)
            dve.wait_ge(w_T_ready, 3)
            def mask_rows(e):
                for m in range(3):
                    wait_reuse(dve, update_ready, 3 * e)
                    nc.vector.tensor_scalar(a_own[m][:, :], a_rows[m][:, :], own[:, bass.ds(e, 1)], None,
                                            ALU.mult).then_inc(own_masked, 1)

            def add_update(e, last):
                for m in range(3):
                    wait_reuse(dve, low_ready, 3 * e)
                    dve.wait_ge(update_ready, 3 * e + m + 1)
                    nc.vector.scalar_tensor_tensor(out=full[m][:, :], in0=psU[m][:, :], scalar=LORA_SCALE,
                                                   in1=w_T[m][:, :], op0=ALU.mult, op1=ALU.add) \
                        .then_inc(full_ready, 1)
                if not last:
                    mask_rows(e + 1)
                for m in range(3):
                    dve.wait_ge(high_ready, 3 * e + m + 1)
                    here = bass.ds(e * F, F)
                    nc.vector.tensor_tensor(w_lo[m][:, here], full[m][:, :], w_hi[m][:, here].bitcast(fp32),
                                            ALU.subtract).then_inc(low_ready, 1)

            mask_rows(0)
            add_update(0, False)
            with dve.Fori(1, E - 1) as e:
                add_update(e, False)
            add_update(E - 1, True)


def routing_block(nc, x_all, xT_all, w_all, gate_dram):
    with ExitStack() as ctx:
        def sb(name, shape, dt=fp32):
            return ctx.enter_context(nc.sbuf_tensor(name, shape, dt))

        def sem(name):
            return ctx.enter_context(nc.semaphore(name))

        ident = sb("ident_r", [P, P])
        stats = sb("stats2", [P, TILES, 6])
        mean, rstd = sb("mean2", [P, TILES]), sb("rstd2", [P, TILES])
        ln_tmp = sb("ln_tmp2", [P, 4, TILES])
        gate = sb("gate", [E, D])
        gate_T = sb("gate_T", [P, E])
        xn = sb("xn2", [P, NT, D])
        xT = sb("xT2", [P, S])
        logits = sb("logits", [P, TILES, E])
        order = sb("order", [P, 1, E])
        pick = [sb(f"pick{k}", [P, TILES, E]) for k in range(2)]
        eq, rest = sb("eq", [P, TILES, E]), sb("rest", [P, TILES, E])
        best = [sb(f"best{k}", [P, TILES]) for k in range(2)]
        first = sb("first", [P, TILES])
        gap, ratio, share = sb("gap", [P, TILES]), sb("ratio", [P, TILES]), [sb(f"share{k}", [P, TILES]) for k in range(2)]
        psX = ctx.enter_context(nc.psum_tensor("psX", [P, S], fp32))
        psG = ctx.enter_context(nc.psum_tensor("psG", [P, 2, S], fp32))
        psL = psG[:, 0, 0:NT * E].rearrange("p (i e) -> p i e", e=E)
        gate_loaded, ident_ready, order_ready, gate_turned, gate_ready = (sem(n) for n in
            ("gate_loaded", "ident_r_ready", "order_ready", "gate_turned", "gate_ready"))
        stats_ready, ln_ready = sem("stats_ready2"), sem("ln_ready2")
        ln_signals = (sem("ln_step2"), sem("var_ready2"), sem("root_ready2"))
        xn_ready, turned, xT_ready, scored, logits_ready = (sem(n) for n in
            ("xn_ready2", "turned2", "xT_ready", "scored", "logits_ready"))
        step, gap_ready, ratio_ready = sem("route_step"), sem("gap_ready"), sem("ratio_ready")
        block = ctx.enter_context(nc.Block())

        @block.sync
        def _(sp):
            sp.dma_start(gate[:, :], gate_dram).then_inc(gate_loaded, 16)

        @block.gpsimd
        def _(pool):
            pool.memset(ident[:, :], 1.0).then_inc(ident_ready, 1)
            pool.wait_ge(ident_ready, 1)
            pool.affine_select(out=ident[:, :], in_=ident[:, :], compare_op=ALU.is_equal, fill=0.0, base=0,
                               pattern=[[-1, P]], channel_multiplier=1).then_inc(ident_ready, 1)
            for e in range(E):
                pool.memset(order[:, 0, e:e + 1], float(E - e)).then_inc(order_ready, 1)

        @block.tensor
        def _(pe):
            pe.wait_ge(ident_ready, 2)
            pe.wait_ge(gate_loaded, 16)
            nc.tensor.transpose(psG[:, 1, 0:E], gate[:, :], ident[0:E, 0:E]).then_inc(gate_turned, 1)
            pe.wait_ge(gate_ready, 1)
            def transpose_and_score(b):
                wait_reuse(pe, xT_ready, 2 * b)
                pe.wait_ge(xn_ready, b + 1)
                for i in range(NT):
                    last = nc.tensor.transpose(psX[:, i * P:(i + 1) * P], xn[:, i, :], ident[:, :])
                last.then_inc(turned, 1)
                wait_reuse(pe, logits_ready, b)
                pe.wait_ge(xT_ready, 2 * b + 1)
                for i in range(NT):
                    last = nc.tensor.matmul(psL[:, i, :], xT[:, i * P:(i + 1) * P], gate_T[:, :],
                                            start=True, stop=True)
                last.then_inc(scored, 1)

            transpose_and_score(0)
            with pe.Fori(1, B) as b:
                transpose_and_score(b)

        @block.scalar
        def _(act):
            row_scales(nc, None, act, stats, mean[:, :], rstd[:, :], ln_tmp, ln_ready, ln_signals)[1]()
            act.wait_ge(gate_turned, 1)
            nc.scalar.activation(gate_T[:, :], psG[:, 1, 0:E], ACT.Copy).then_inc(gate_ready, 1)
            def copy_out(b):
                wait_reuse(act, scored, b)
                act.wait_ge(turned, b + 1)
                nc.scalar.activation(xT[:, :], psX[:, :], ACT.Copy).then_inc(xT_ready, 1)
                nc.scalar.activation(xT_all[:, bass.ds(b * S, S)], psX[:, :], ACT.Copy).then_inc(xT_ready, 1)
                act.wait_ge(gate_ready, 1)
                act.wait_ge(scored, b + 1)
                nc.scalar.activation(logits[:, bass.ds(b * NT, NT), :], psL, ACT.Copy).then_inc(logits_ready, 1)

            copy_out(0)
            with act.Fori(1, B) as b:
                copy_out(b)
            act.wait_ge(gap_ready, 1)
            nc.scalar.activation(ratio[:, :], gap[:, :], ACT.Exp).then_inc(ratio_ready, 1)

        @block.vector
        def _(dve):
            for i in range(TILES):
                last = nc.vector.bn_stats(stats[:, i, :], x_all[:, i, :])
            last.then_inc(stats_ready, 1)
            dve.wait_ge(stats_ready, 1)
            row_scales(nc, dve, None, stats, mean[:, :], rstd[:, :], ln_tmp, ln_ready, ln_signals)[0]()
            def normalise_tokens(b):
                wait_reuse(dve, turned, b)
                for i in range(NT):
                    last = nc.vector.tensor_scalar(
                        xn[:, i, :], x_all[:, bass.ds(b * NT + i, 1), :].rearrange("p i d -> p (i d)"),
                        mean[:, bass.ds(b * NT + i, 1)], rstd[:, bass.ds(b * NT + i, 1)],
                        ALU.subtract, ALU.mult)
                last.then_inc(xn_ready, 1)

            normalise_tokens(0)
            with dve.Fori(1, B) as b:
                normalise_tokens(b)
            n = [0]

            def then(ins):
                n[0] += 1
                ins.then_inc(step, 1)
                dve.wait_ge(step, n[0])

            def wide(v):
                return v.unsqueeze(2).broadcast_to([P, TILES, E])

            dve.wait_ge(logits_ready, B)
            dve.wait_ge(order_ready, E)
            left = logits
            for k in range(2):
                then(nc.vector.tensor_reduce(out=best[k][:, :], in_=left[:, :, :], op=ALU.max, axis=AX.X))
                then(nc.vector.tensor_tensor(eq[:, :, :], left[:, :, :], wide(best[k][:, :]), ALU.is_equal))
                then(nc.vector.tensor_tensor(eq[:, :, :], eq[:, :, :], order[:, :, :].broadcast_to([P, TILES, E]),
                                             ALU.mult))
                then(nc.vector.tensor_reduce(out=first[:, :], in_=eq[:, :, :], op=ALU.max, axis=AX.X))
                then(nc.vector.tensor_tensor(pick[k][:, :, :], eq[:, :, :], wide(first[:, :]), ALU.is_equal))
                if k == 0:
                    then(nc.vector.tensor_scalar(rest[:, :, :], pick[0][:, :, :], -3e38, None, ALU.mult))
                    then(nc.vector.tensor_tensor(rest[:, :, :], rest[:, :, :], logits[:, :, :], ALU.add))
                    left = rest
            nc.vector.tensor_tensor(gap[:, :], best[1][:, :], best[0][:, :], ALU.subtract).then_inc(gap_ready, 1)
            dve.wait_ge(ratio_ready, 1)
            then(nc.vector.tensor_scalar(share[1][:, :], ratio[:, :], 1.0, None, ALU.add))
            then(nc.vector.reciprocal(share[0][:, :], share[1][:, :]))
            then(nc.vector.tensor_tensor(share[1][:, :], ratio[:, :], share[0][:, :], ALU.mult))
            then(nc.vector.tensor_tensor(eq[:, :, :], pick[0][:, :, :], wide(share[0][:, :]), ALU.mult))
            then(nc.vector.tensor_tensor(rest[:, :, :], pick[1][:, :, :], wide(share[1][:, :]), ALU.mult))
            then(nc.vector.tensor_tensor(w_all[:, :, :], eq[:, :, :], rest[:, :, :], ALU.add))


def experts_block(nc, x_all, xT_all, w_all, w_hi, w_lo, out_dram):
    units = E * FC
    with ExitStack() as ctx:
        def sb(name, shape, dt=fp32):
            return ctx.enter_context(nc.sbuf_tensor(name, shape, dt))

        def sem(name):
            return ctx.enter_context(nc.semaphore(name))

        ident = sb("ident_e", [P, P])
        x_hi, x_lo = sb("x_hi", [P, 2, S], f32r), sb("x_lo", [P, 2, S], f32r)
        w_wide = sb("w_wide", [P, 2, NT, P])
        xw = sb("xw", [P, S])
        xw_hi = [sb(f"xw_hi{i}", [P, S], f32r) for i in range(2)]
        xw_lo = [sb(f"xw_lo{i}", [P, S], f32r) for i in range(2)]
        gated = [sb(f"gated{i}", [P, S]) for i in range(2)]
        hidden = [sb(f"hidden{i}", [P, S]) for i in range(4)]
        hid_hi = [sb(f"hid_hi{i}", [P, S], f32r) for i in range(4)]
        hid_lo = [sb(f"hid_lo{i}", [P, S], f32r) for i in range(4)]
        yT = sb("yT", [P, S])
        psH = ctx.enter_context(nc.psum_tensor("psH", [P, 2, S], fp32))
        psU = ctx.enter_context(nc.psum_tensor("psUp", [P, 2, S], fp32))
        psY = ctx.enter_context(nc.psum_tensor("psY", [P, S], fp32))
        psW = ctx.enter_context(nc.psum_tensor("psW", [P, S], fp32))
        psO = ctx.enter_context(nc.psum_tensor("psO", [P, S], fp32))
        (ident_ready, x_high, x_ready, wide_ready, wide_turned, xw_made, xw_high, xw_ready, gate_done, up_done,
         gated_ready, hidden_ready, hid_high, hid_low, down_done, yT_ready, y_turned, result_ready,
         stored) = (sem(n) for n in
            ("ident_e_ready", "x_high", "x_ready", "wide_ready", "wide_turned", "xw_made", "xw_high", "xw_ready",
             "gate_done", "up_done", "gated_ready", "hidden_ready", "hid_high", "hid_low", "down_done",
             "yT_ready", "y_turned", "result_ready", "stored"))
        block = ctx.enter_context(nc.Block())

        @block.sync
        def _(sp):
            with sp.Fori(0, B) as b:
                sp.wait_ge(result_ready, b + 1)
                sp.dma_start(out_dram[bass.ds(b, 1)].rearrange("b (i p) d -> p (b i) d", p=P),
                             x_all[:, bass.ds(b * NT, NT), :]) \
                    .then_inc(stored, 16)
            sp.wait_ge(stored, 16 * B)


        @block.gpsimd
        def _(pool):
            pool.memset(ident[:, :], 1.0).then_inc(ident_ready, 1)
            pool.wait_ge(ident_ready, 1)
            pool.affine_select(out=ident[:, :], in_=ident[:, :], compare_op=ALU.is_equal, fill=0.0, base=0,
                               pattern=[[-1, P]], channel_multiplier=1).then_inc(ident_ready, 1)

            def widen(b, e):
                wait_reuse(pool, wide_turned, E * b + e - 1)
                pool.tensor_copy(w_wide[:, e % 2, :, :],
                                 w_all[:, bass.ds(b * NT, NT), e:e + 1].broadcast_to([P, NT, P])) \
                    .then_inc(wide_ready, 1)

            def group(b, last):
                for u in range(units):
                    n = units * b + u
                    if u % FC == 0 and u // FC + 2 < E:
                        widen(b, u // FC + 2)
                    elif u % FC == 0 and not last:
                        widen(b + 1, u // FC + 2 - E)
                    pool.wait_ge(hid_high, n + 1)
                    pool.tensor_tensor(hid_lo[u % 4][:, :], hidden[u % 4][:, :],
                                       hid_hi[u % 4][:, :].bitcast(fp32), ALU.subtract).then_inc(hid_low, 1)

            widen(0, 0)
            widen(0, 1)
            group(0, False)
            with pool.Fori(1, B - 1) as b:
                group(b, False)
            group(B - 1, True)

        @block.scalar
        def _(act):
            def high(n, slot):
                wait_reuse(act, down_done, n - 3)
                act.wait_ge(hidden_ready, n + 1)
                nc.scalar.activation(hid_hi[slot][:, :], hidden[slot][:, :], ACT.Copy).then_inc(hid_high, 1)

            def copy_y(b):
                act.wait_ge(down_done, units * b + units)
                nc.scalar.activation(yT[:, :], psY[:, :], ACT.Copy).then_inc(yT_ready, 1)

            def group(b, first):
                for u in range(units):
                    n = units * b + u
                    act.wait_ge(gate_done, n + 1)
                    wait_reuse(act, hidden_ready, n - 1)
                    nc.scalar.activation(gated[u % 2][:, :], psH[:, u % 2, :], ACT.Silu).then_inc(gated_ready, 1)
                    if u > 0 or not first:
                        high(n - 1, (u - 1) % 4)
                    if u == 2 and not first:
                        copy_y(b - 1)

            group(0, True)
            with act.Fori(1, B) as b:
                group(b, False)
            high(units * B - 1, 3)
            copy_y(B - 1)

        @block.vector
        def _(dve):
            def split_x(b, slot):
                here = xT_all[:, bass.ds(b * S, S)]
                hi, lo = x_hi[:, bass.ds(slot, 1), :], x_lo[:, bass.ds(slot, 1), :]
                nc.vector.tensor_copy(hi.rearrange("p a s -> p (a s)"), here).then_inc(x_high, 1)
                dve.wait_ge(x_high, b + 1)
                nc.vector.tensor_tensor(lo.rearrange("p a s -> p (a s)"), here,
                                        hi.rearrange("p a s -> p (a s)").bitcast(fp32),
                                        ALU.subtract).then_inc(x_ready, 1)

            def weigh(b, e):
                slot = e % 2
                wait_reuse(dve, up_done, units * b + FC * e - FC)
                wait_reuse(dve, xw_ready, E * b + e)
                dve.wait_ge(wide_turned, E * b + e + 1)
                nc.vector.tensor_tensor(xw[:, :], psW[:, :], xT_all[:, bass.ds(b * S, S)], ALU.mult) \
                    .then_inc(xw_made, 1)
                dve.wait_ge(xw_made, E * b + e + 1)
                nc.vector.tensor_copy(xw_hi[slot][:, :], xw[:, :]).then_inc(xw_high, 1)

            def weigh_low(b, e):
                slot = e % 2
                dve.wait_ge(xw_high, E * b + e + 1)
                nc.vector.tensor_tensor(xw_lo[slot][:, :], xw[:, :], xw_hi[slot][:, :].bitcast(fp32),
                                        ALU.subtract).then_inc(xw_ready, 1)

            def add_result(b):
                dve.wait_ge(y_turned, b + 1)
                here = x_all[:, bass.ds(b * NT, NT), :]
                nc.vector.tensor_tensor(here, psO[:, :].rearrange("p (i d) -> p i d", d=D), here,
                                        ALU.add).then_inc(result_ready, 1)

            def group(b, first, last):
                for u in range(units):
                    n = units * b + u
                    dve.wait_ge(gated_ready, n + 1)
                    dve.wait_ge(up_done, n + 1)
                    wait_reuse(dve, hid_low, n - 3)
                    nc.vector.tensor_tensor(hidden[u % 4][:, :], gated[u % 2][:, :], psU[:, u % 2, :],
                                            ALU.mult).then_inc(hidden_ready, 1)
                    if u // FC + 1 < E:
                        if u % FC == 1:
                            weigh(b, u // FC + 1)
                        elif u % FC == 2:
                            weigh_low(b, u // FC + 1)
                    elif not last:
                        if u % FC == 0:
                            split_x(b + 1, (b + 1) % 2)
                        elif u % FC == 1:
                            weigh(b + 1, 0)
                        elif u % FC == 2:
                            weigh_low(b + 1, 0)
                    if u == 7 and not first:
                        add_result(b - 1)

            split_x(0, 0)
            weigh(0, 0)
            weigh_low(0, 0)
            group(0, True, False)
            with dve.Fori(1, B - 1) as b:
                group(b, False, False)
            group(B - 1, False, True)
            add_result(B - 1)

        @block.tensor
        def _(pe):
            pe.wait_ge(ident_ready, 2)

            def turn_weights(b, e):
                wait_reuse(pe, xw_made, E * b + e)
                pe.wait_ge(wide_ready, E * b + e + 1)
                for i in range(NT):
                    last = nc.tensor.transpose(psW[:, i * P:(i + 1) * P], w_wide[:, e % 2, i, :], ident[:, :])
                last.then_inc(wide_turned, 1)

            def product(out, m, u, hi, lo, start, stop):
                at = slice(u * P, (u + 1) * P)
                nc.tensor.matmul(out, w_hi[m][:, at], hi, start=start, stop=False)
                nc.tensor.matmul(out, w_hi[m][:, at], lo, start=False, stop=False)
                return nc.tensor.matmul(out, w_lo[m][:, at], hi, start=False, stop=stop)

            def down(n, u):
                pe.wait_ge(hid_low, n + 1)
                product(psY[:, :], 2, u, hid_hi[u % 4][:, :], hid_lo[u % 4][:, :], u == 0, u == units - 1) \
                    .then_inc(down_done, 1)

            def turn_y(b):
                pe.wait_ge(yT_ready, b + 1)
                for i in range(NT):
                    last = nc.tensor.transpose(psO[:, i * P:(i + 1) * P], yT[:, i * P:(i + 1) * P], ident[:, :])
                last.then_inc(y_turned, 1)

            def group(b, slot, first, last):
                here = bass.ds(slot, 1)
                hi = x_hi[:, here, :].rearrange("p a s -> p (a s)")
                lo = x_lo[:, here, :].rearrange("p a s -> p (a s)")
                pe.wait_ge(x_ready, b + 1)
                for u in range(units):
                    n = units * b + u
                    s = u % 2
                    wait_reuse(pe, gated_ready, n - 1)
                    product(psH[:, s, :], 0, u, hi, lo, True, True).then_inc(gate_done, 1)
                    wait_reuse(pe, hidden_ready, n - 1)
                    if u % FC == 0:
                        pe.wait_ge(xw_ready, E * b + u // FC + 1)
                    e = u // FC
                    product(psU[:, s, :], 1, u, xw_hi[e % 2][:, :], xw_lo[e % 2][:, :], True, True) \
                        .then_inc(up_done, 1)
                    if u % FC == 0 and e + 1 < E:
                        turn_weights(b, e + 1)
                    elif u % FC == 0 and not last:
                        turn_weights(b + 1, 0)
                    if u >= 3:
                        if u == 3 and not first:
                            pe.wait_ge(yT_ready, b)
                        down(n - 3, u - 3)
                    elif not first:
                        down(n - 3, units + u - 3)
                    if u == 5 and not first:
                        turn_y(b - 1)

            turn_weights(0, 0)
            group(0, 0, True, False)
            with pe.Fori(1, B - 1) as b:
                group(b, b % 2, False, False)
            group(B - 1, (B - 1) % 2, False, True)
            down(units * B - 3, units - 3)
            down(units * B - 2, units - 2)
            down(units * B - 1, units - 1)
            turn_y(B - 1)


def layer(nc, x_dram, wq_dram, wkv_dram, wo_dram, gate_dram, w_gate_dram, w_up_dram, w_down_dram,
          a1_dram, b1_dram, a3_dram, b3_dram, a2_dram, b2_dram, rope_q_dram, rope_k_dram, mask_dram,
          out_dram):
    with ExitStack() as ctx:
        def sb(name, shape, dt):
            return ctx.enter_context(nc.sbuf_tensor(name, shape, dt))

        x_all = sb("x_all", [P, TILES, D], fp32)
        attention_block(nc, x_all, x_dram, wq_dram, wkv_dram, wo_dram, rope_q_dram, rope_k_dram, mask_dram)
        w_hi = [sb(f"w_hi{m}", [P, E * F], f32r) for m in range(3)]
        w_lo = [sb(f"w_lo{m}", [P, E * F], f32r) for m in range(3)]
        expert_weights_block(nc, w_hi, w_lo, (w_gate_dram, w_up_dram, w_down_dram),
                             (a1_dram, a3_dram, a2_dram), (b1_dram, b3_dram, b2_dram))
        xT_all = sb("xT_all", [P, B * S], fp32)
        w_all = sb("w_all", [P, TILES, E], fp32)
        routing_block(nc, x_all, xT_all, w_all, gate_dram)
        experts_block(nc, x_all, xT_all, w_all, w_hi, w_lo, out_dram)


def rope_tables():
    inv_freq = (np.float32(1.0) / np.float32(10000.0) ** (np.arange(0, DH, 2, dtype=np.float32)
                                                         / np.float32(DH))).astype(np.float32)
    freqs = np.arange(S, dtype=np.float32)[:, None] * inv_freq[None, :]
    angle = np.concatenate([freqs, freqs], axis=-1).astype(np.float32)
    cos, sin = np.cos(angle), np.sin(angle)
    sin_q = np.concatenate([sin[:, :HALF], -sin[:, HALF:]], axis=-1)
    scale = np.float32(DH ** -0.5)
    by_token = [np.repeat((t * scale).reshape(NT, P, 1, DH), 2, axis=2).transpose(1, 0, 2, 3).reshape(P, -1)
                for t in (cos, sin_q)]
    sin_k = np.concatenate([-sin[:, :HALF], sin[:, HALF:]], axis=-1)
    by_row = [np.concatenate([t.T, t.T], axis=0) for t in (cos, sin_k)]
    return (np.ascontiguousarray(np.stack(by_token, axis=1).astype(np.float32)),
            np.ascontiguousarray(np.stack(by_row, axis=1).astype(np.float32)))


_INS = ['L0_attn_x', 'L0_attn_Wq', 'L0_attn_Wkv', 'L0_attn_Wo', 'L0_ffn_gate_w', 'L0_ffn_w_gate',
        'L0_ffn_w_up', 'L0_ffn_w_down', 'L0_ffn_A1', 'L0_ffn_B1', 'L0_ffn_A3', 'L0_ffn_B3', 'L0_ffn_A2',
        'L0_ffn_B2']


def kernel(**inputs):
    import ml_dtypes
    import concourse.bacc as bacc
    from concourse.bass_utils import run_bass_kernel_spmd

    nc = bacc.Bacc("TRN2", target_bir_lowering=False, num_devices=1)
    arrays, args = {}, []
    for name in _INS:
        a = np.ascontiguousarray(inputs[name])
        arrays[f"in_{name}"] = a
        args.append(nc.dram_tensor(f"in_{name}", a.shape, mybir.dt.from_np(a.dtype), kind="ExternalInput").ap())
    rope_q, rope_k = rope_tables()
    mask = np.triu(np.full((P, P), MASKED, np.float32), k=1).astype(ml_dtypes.bfloat16)
    for name, a in (("rope_q", rope_q), ("rope_k", rope_k), ("mask", mask)):
        arrays[name + "_const"] = a
        args.append(nc.dram_tensor(name + "_const", a.shape, mybir.dt.from_np(a.dtype), kind="ExternalInput").ap())
    args.append(nc.dram_tensor("out", (B, S, D), fp32, kind="ExternalOutput").ap())
    layer(nc, *args)
    r = run_bass_kernel_spmd(nc, [arrays], core_ids=[0])
    return r.results[0]["out"]
```
